# Optimizing a Trainium2 kernel written in Bass

```python
import numpy as np
import jax
import jax.numpy as jnp

def _softmax(x, axis=-1):
    return jax.nn.softmax(x, axis=axis)

def _gelu(x):
    return jax.nn.gelu(x, approximate=True)

def _silu(x):
    return jax.nn.silu(x)

def _sigmoid(x):
    return jax.nn.sigmoid(x)

def _layernorm(x, axis=-1, eps=1e-05):
    m = jnp.mean(x, axis=axis, keepdims=True)
    v = jnp.var(x, axis=axis, keepdims=True)
    return (x - m) / jnp.sqrt(v + eps)

def _scatter_add(tgt, idx, src, axis=0):
    return tgt.at[idx].add(src)

def _segment_sum(src, seg, n):
    return jax.ops.segment_sum(src, seg, n)
kernel_name = 'mk_rec_standalone_d1_rec_r8_242de6'

def setup_inputs(seed: int=0):
    np.random.seed(seed)
    _w = jnp.asarray

    def _rec_inputs():
        import jax
        import jax.numpy as jnp
        _rk = jax.random.key(seed)
        r_x = -0.000718957 + 1.00057 * jax.random.normal(jax.random.fold_in(_rk, 1), (512, 40, 32), jnp.float32)
        return r_x
    r_x = _rec_inputs()

    def _L0_rec_setup():
        import jax, jax.numpy as jnp
        import numpy as np
        B, F0, D = (256, 40, 32)
        LAYER0, LAYER1 = (128, 128)
        key = jax.random.key(seed)
        k1, k2, k3 = jax.random.split(key, 3)
        x = jax.random.normal(k1, (B, F0, D), dtype=jnp.float32)
        W0 = jax.random.normal(k2, (F0, F0, LAYER0), dtype=jnp.float32) * 0.05
        b0 = jnp.zeros((LAYER0,), dtype=jnp.float32)
        W1 = jax.random.normal(k3, (F0, LAYER0 // 2, LAYER1), dtype=jnp.float32) * 0.05
        b1 = jnp.zeros((LAYER1,), dtype=jnp.float32)
        return {'x': x, 'W0': W0, 'b0': b0, 'W1': W1, 'b1': b1}
    _L0_rec_all = _L0_rec_setup()
    _L0_rec_in = {k: v for k, v in _L0_rec_all.items() if k in ('W0', 'b0', 'W1', 'b1')}
    del _L0_rec_all
    return {'r_x': r_x, 'L0_rec_W0': _L0_rec_in['W0'], 'L0_rec_b0': _L0_rec_in['b0'], 'L0_rec_W1': _L0_rec_in['W1'], 'L0_rec_b1': _L0_rec_in['b1']}

def reference(r_x, L0_rec_W0, L0_rec_b0, L0_rec_W1, L0_rec_b1):
    import jax
    import jax.numpy as jnp

    def _L0_rec_ref(x, W0, b0, W1, b1):
        import jax, jax.numpy as jnp
        import numpy as np
        B, F0, D = (256, 40, 32)
        LAYER0, LAYER1 = (128, 128)
        h0 = jax.nn.relu(jnp.einsum('bid,bjd,ijs->bsd', x, x, W0) + b0[None, :, None])
        half = LAYER0 // 2
        next_hidden, direct0 = (h0[:, :half, :], h0[:, half:, :])
        direct1 = jax.nn.relu(jnp.einsum('bid,bjd,ijs->bsd', x, next_hidden, W1) + b1[None, :, None])
        result = jnp.concatenate([direct0, direct1], axis=1)
        return jnp.sum(result, axis=-1)
    y = _L0_rec_ref(r_x, L0_rec_W0, L0_rec_b0, L0_rec_W1, L0_rec_b1)
    return y

_drawn_inputs = setup_inputs


def setup_inputs(seed=0):
    import zlib

    import numpy as np

    out = dict(_drawn_inputs(seed))
    spreads = {'L0_rec_b0': (0.0, 0.312), 'L0_rec_b1': (0.0, 0.1)}
    factors = {}
    for name, (base, spread) in spreads.items():
        noise = np.random.default_rng([zlib.crc32(name.encode()), seed]).standard_normal(out[name].shape)
        drawn = base * np.exp(spread * noise) if base else spread * noise
        out[name] = jnp.asarray(drawn.astype(out[name].dtype))
    for name, factor in factors.items():
        out[name] = (out[name] * factor).astype(out[name].dtype)
    return out
```

```python
from contextlib import ExitStack

import numpy as np

import concourse.bass as bass
from concourse import mybir

B, F, D = 512, 40, 32
S0, S1 = 128, 128
HALF = S0 // 2
N = B * D
NC = 512
CHUNKS = N // NC
BC = NC // D
ROT = 128 // F
K0 = ROT * F
T0 = (F // 2 + 1) // ROT
K1 = 128
T1 = F * HALF // K1
GROUPS = 4
FG = F // GROUPS
TG = T1 // GROUPS
FR = 16
FSTEP = 8

POOL, DVE, NATIVE = "pool", "dve", "native"
LAG = 3
SLOTS = 7
RING = 3

def _a(i, mode):
    return [(0, 0, tuple(t for t in (2 * i, 2 * i + 1) if t < T0), mode)]


def _s(u, mode_a, mode_b):
    return [(1, 0, (u, TG + u), mode_a), (1, 2, (2 * TG + u, 3 * TG + u), mode_b)]


STEPS0 = [_a(0, POOL), _a(1, NATIVE), _a(2, NATIVE), _a(3, NATIVE)]
STEPS1 = [_s(0, POOL, POOL), _s(1, POOL, POOL), _s(2, POOL, POOL), _s(3, POOL, NATIVE), _s(4, POOL, NATIVE)]
FIRST = STEPS0
FULL = [STEPS0[0], STEPS1[0], STEPS0[1], STEPS1[1], STEPS0[2],
        STEPS1[2], STEPS0[3], STEPS1[3], STEPS1[4]]
LAST = STEPS1
PHASES = {"first": FIRST, "full": FULL, "last": LAST}
WAYS = (POOL, DVE, NATIVE)
LAYER0_END = 1 + max(k for k, p in enumerate(x for step in FULL for x in step) if p[0] == 0)


def pairs(phase):
    return [p for step in PHASES[phase] for p in step]


def counted(phase, k, ways):
    return sum(p[3] in ways for p in pairs(phase)[:k])


def done(c, phase, k, ways=WAYS):
    if phase == "first":
        return counted(phase, k, ways)
    return counted("full", 99, ways) * c + (counted("first", 99, ways) + counted(phase, k, ways))


def step_start(phase, s):
    return sum(len(x) for x in PHASES[phase][:s])


def slot(u, phase, k):
    return k % SLOTS if phase == "first" else (4 + 14 * (1 + u) + k) % SLOTS


def sel_tables():
    rot = np.zeros((128, T0, 128), np.float32)
    rep = np.zeros((128, TG, 128), np.float32)
    for q in range(T0):
        for p in range(K0):
            f = (p // ROT + ROT * q + p % ROT) % F
            g = f // FG
            for half in range(2):
                rot[32 * g + 2 * (f - FSTEP * g) + half, q, p] = 1
    for g in range(GROUPS):
        for u in range(TG):
            for p in range(K1):
                f = 2 * (TG * g + u) + p // HALF
                for half in range(2):
                    rep[32 * g + 2 * (f - FSTEP * g) + half, u, p] = 1
    p = np.arange(128)
    flags = np.stack([p % 2 == 1, p % ROT > 0, p % ROT < ROT - 1], 1).astype(np.float32)
    return np.concatenate([rot, rep], 1), flags


def build(nc, xT, w0_ij, w0_ji, w1, b0, b1, sel_dram, flags_dram, yT):
    f32, f32r = mybir.dt.float32, mybir.dt.float32r
    ALU, ACT = mybir.AluOpType, mybir.ActivationFunctionType
    T = T0 + T1
    NSEL = T0 + TG
    with ExitStack() as ctx:
        def sb(name, shape, dt=f32):
            return ctx.enter_context(nc.sbuf_tensor(name, shape, dt))

        def sem(name):
            return ctx.enter_context(nc.semaphore(name))

        w_in = sb("w_in", [128, T, S0])
        w0_back = sb("w0_back", [128, T0, S0])
        w = sb("w", [128, T0, S0])
        w_hi = sb("w_hi", [128, T, S0], f32r)
        w_lo = sb("w_lo", [128, T, S0], f32r)
        sel_in = sb("sel_in", [128, NSEL, 128])
        sel = sb("sel", [128, NSEL, 128], f32r)
        flags = sb("flags", [128, 3])
        bias0 = sb("bias0", [128, 1])
        bias0h = sb("bias0h", [128, 1])
        bias1 = sb("bias1", [128, 1])
        x_rows = sb("x_rows", [128, RING, NC])
        x_cut = sb("x_cut", [128, NC], f32r)
        x_half = sb("x_half", [128, RING, NC], f32r)
        x_left = sb("x_left", [128, RING, NC])
        h = sb("h", [128, RING, NC])
        direct0 = sb("direct0", [128, RING, NC])
        direct1 = sb("direct1", [128, RING, NC])
        prod = sb("prod", [128, SLOTS, 2, NC])
        prod_hi = sb("prod_hi", [128, SLOTS, 2, NC], f32r)
        prod_lo = sb("prod_lo", [128, SLOTS, 2, NC], f32r)
        y0 = sb("y0", [128, B])
        y1 = sb("y1", [128, B])
        bc1 = ctx.enter_context(nc.psum_tensor("bc1", [128, GROUPS, NC], f32))
        bc0 = ctx.enter_context(nc.psum_tensor("bc0", [128, 2, NC], f32))
        acc0 = ctx.enter_context(nc.psum_tensor("acc0", [128, NC], f32))
        acc1 = ctx.enter_context(nc.psum_tensor("acc1", [128, NC], f32))

        sel_loaded = sem("sel_loaded")
        w0_loaded, w1_loaded, bias_loaded = sem("w0_loaded"), sem("w1_loaded"), sem("bias_loaded")
        x_rows_loaded = [sem(f"x_rows_loaded{i}") for i in range(RING)]
        x_left_loaded = [sem(f"x_left_loaded{i}") for i in range(RING)]
        sel_ready = sem("sel_ready")
        w0_summed, w0_hi_ready, w0_ready = sem("w0_summed"), sem("w0_hi_ready"), sem("w0_ready")
        w1_hi_ready, w1_ready = sem("w1_hi_ready"), sem("w1_ready")
        x_cut_ready = sem("x_cut_ready")
        x_half_ready = sem("x_half_ready")
        bc_ready = sem("bc_ready")
        prod_ready = sem("prod_ready")
        hi_ready = sem("hi_ready")
        lo_ready = sem("lo_ready")
        dve_lo_ready = sem("dve_lo_ready")
        pair_done = sem("pair_done")
        h_ready = sem("h_ready")
        direct0_ready = sem("direct0_ready")
        direct1_ready = sem("direct1_ready")
        y_ready = sem("y_ready")
        y_stored = sem("y_stored")
        block = ctx.enter_context(nc.Block())

        def weight(t):
            return w[:K0, t, :] if t < T0 else w_in[:, t, :]

        def chunks(engine, chunk):
            chunk(-1, -2, 0, "first")
            chunk(0, -1, 0, "full")
            loops = (CHUNKS - 2) // RING - 1
            with engine.Fori(0, loops) as it:
                for u in range(RING):
                    chunk(it * RING + (1 + u), u, it, "full")
            for c in range(1 + RING * loops, CHUNKS - 1):
                chunk(c, (c - 1) % RING, (c - 1) // RING, "full")
            chunk(CHUNKS - 1, (CHUNKS - 2) % RING, (CHUNKS - 2) // RING, "last")

        def ring(u, ahead=0):
            return (1 + u + ahead) % RING

        def filling(u, it, ahead):
            return it + ((1 + u + ahead) // RING + 1)

        @block.sync
        def _(sp):
            def load_chunk(c, i):
                x_of = xT[:, bass.ds(c * NC, NC)].unsqueeze(1)
                for g in range(GROUPS):
                    sp.dma_start(x_rows[32 * g:32 * g + 32, i, :],
                                 x_of[FSTEP * g:FSTEP * g + FR].broadcast_to([FR, 2, NC])).then_inc(x_rows_loaded[i], 16)
                sp.dma_start(x_left[:K0, i, :], x_of.broadcast_to([F, ROT, NC])).then_inc(x_left_loaded[i], 16)

            sp.dma_start(sel_in[:], sel_dram).then_inc(sel_loaded, 16)
            load_chunk(0, 0)
            load_chunk(1, 1)
            load_chunk(2, 2)

            def refill(c, i):
                sp.wait_ge(x_half_ready, c - (RING - 1))
                sp.wait_ge(prod_ready, done(c - (RING + 1), "full", 14))
                load_chunk(c, i)

            loops = (CHUNKS - RING - 1) // RING
            refill(RING, 0)
            with sp.Fori(0, loops) as it:
                for u in range(RING):
                    refill(it * RING + (RING + 1 + u), (1 + u) % RING)
            for c in range(RING + 1 + RING * loops, CHUNKS):
                refill(c, c % RING)
            sp.wait_ge(y_ready, 1)
            sp.dma_start(yT[:HALF, :], y0[HALF:, :]).then_inc(y_stored, 16)
            sp.dma_start(yT[HALF:, :], y1[:]).then_inc(y_stored, 16)
            sp.wait_ge(y_stored, 32)

        @block.gpsimd
        def _(pool):
            def halve(c, i):
                pool.wait_ge(x_cut_ready, c + 1)
                nc.gpsimd.tensor_tensor(x_half[:, i, :], x_rows[:, i, :], x_cut[:].bitcast(f32),
                                        ALU.subtract).then_inc(x_half_ready, 1)

            halve(0, 0)
            halve(1, 1)

            def chunk(c, u, it, phase):
                for k, (layer, bank, tiles, mode) in enumerate(pairs(phase)):
                    if mode == POOL:
                        s, rows, nt = slot(u, phase, k), K0 if layer == 0 else K1, len(tiles)
                        pool.wait_ge(hi_ready, done(c, phase, k + 1, (POOL, DVE)))
                        nc.gpsimd.tensor_tensor(prod_lo[:rows, s, :nt, :], prod[:rows, s, :nt, :],
                                                prod_hi[:rows, s, :nt, :].bitcast(f32),
                                                ALU.subtract).then_inc(lo_ready, 1)
                    if phase == "full" and k == X_AT and not (isinstance(c, int) and c + 2 >= CHUNKS):
                        pool.wait_ge(bc_ready, done(c, phase, k))
                        halve(c + 2, ring(u, 2))

            chunks(pool, chunk)

        @block.scalar
        def _(act):
            act.dma_start(w_in[:K0, :T0, :], w0_ij).then_inc(w0_loaded, 16)
            act.dma_start(w0_back[:K0], w0_ji).then_inc(w0_loaded, 16)
            act.dma_start(flags[:], flags_dram).then_inc(bias_loaded, 16)
            act.dma_start(bias0[:], b0).then_inc(bias_loaded, 16)
            act.dma_start(bias0h[:HALF], b0[:HALF]).then_inc(bias_loaded, 16)
            act.dma_start(bias0h[HALF:], b0[:HALF]).then_inc(bias_loaded, 16)
            act.dma_start(bias1[:], b1).then_inc(bias_loaded, 16)
            act.dma_start(w_in[:, T0:, :], w1).then_inc(w1_loaded, 16)

            def cut(c, i, times):
                act.wait_ge(x_rows_loaded[i], times * (16 * GROUPS))
                if not isinstance(c, int) or c > 0:
                    act.wait_ge(x_half_ready, c)
                nc.scalar.activation(x_cut[:], x_rows[:, i, :], ACT.Copy, scale=flags[:, 0:1]).then_inc(x_cut_ready, 1)

            act.wait_ge(bias_loaded, 80)
            cut(0, 0, 1)
            act.wait_ge(sel_loaded, 16)
            nc.scalar.copy(sel[:], sel_in[:]).then_inc(sel_ready, 1)
            act.wait_ge(w0_summed, 1)
            nc.scalar.copy(w_hi[:K0, :T0, :], w[:K0, :, :]).then_inc(w0_hi_ready, 1)
            cut(1, 1, 1)

            def read_acc0(c, u):
                if isinstance(c, int) and c == 0:
                    act.wait_ge(pair_done, done(-1, "first", len(pairs("first"))))
                else:
                    act.wait_ge(pair_done, done(c - 1, "full", LAYER0_END))
                i = ring(u)
                nc.scalar.activation(h[:HALF, i, :], acc0[:HALF, :], ACT.Relu, bias=bias0h[:HALF])
                nc.scalar.activation(h[HALF:, i, :], acc0[:HALF, :], ACT.Relu, bias=bias0h[HALF:]).then_inc(h_ready, 1)
                nc.scalar.activation(direct0[HALF:, i, :], acc0[HALF:, :], ACT.Relu, bias=bias0[HALF:]).then_inc(direct0_ready, 1)

            def read_acc1(c, u, phase="full", k=14):
                act.wait_ge(pair_done, done(c, phase, k))
                nc.scalar.activation(direct1[:, ring(u), :], acc1[:], ACT.Relu, bias=bias1[:]).then_inc(direct1_ready, 1)

            def chunk(c, u, it, phase):
                for k, (layer, bank, tiles, mode) in enumerate(pairs(phase)):
                    if phase != "first" and k == (1 if phase == "full" else 0):
                        read_acc0(c, u)
                    if mode != NATIVE:
                        s, rows, nt = slot(u, phase, k), K0 if layer == 0 else K1, len(tiles)
                        act.wait_ge(prod_ready, done(c, phase, k + 1))
                        nc.scalar.copy(prod_hi[:rows, s, :nt, :], prod[:rows, s, :nt, :]).then_inc(hi_ready, 1)
                    if phase != "first" and k == ACC1_AT and not (isinstance(c, int) and c == 0):
                        read_acc1(c - 1, u - 1)
                    if phase == "full" and k == X_AT and not (isinstance(c, int) and c + 2 >= CHUNKS):
                        cut(c + 2, ring(u, 2), filling(u, it, 2))
                if phase == "first":
                    act.wait_ge(w1_loaded, 16)
                    nc.scalar.copy(w_hi[:, T0:, :], w_in[:, T0:, :]).then_inc(w1_hi_ready, 1)
                if phase == "last":
                    read_acc1(c, u, "last", 10)

            chunks(act, chunk)

        @block.vector
        def _(dve):
            dve.wait_ge(w0_loaded, 32)
            dve.wait_ge(bias_loaded, 80)
            for t, flag in ((0, 1), (T0 - 1, 2)):
                nc.vector.scalar_tensor_tensor(w[:K0, t, :], w0_back[:K0, t, :], flags[:K0, flag:flag + 1],
                                               w_in[:K0, t, :], ALU.mult, ALU.add)
            nc.vector.tensor_tensor(w[:K0, 1:T0 - 1, :], w_in[:K0, 1:T0 - 1, :], w0_back[:K0, 1:T0 - 1, :],
                                    ALU.add).then_inc(w0_summed, 1)
            dve.wait_ge(w0_hi_ready, 1)
            nc.vector.tensor_tensor(w_lo[:K0, :T0, :], w[:K0, :, :], w_hi[:K0, :T0, :].bitcast(f32),
                                    ALU.subtract).then_inc(w0_ready, 1)

            def reduce0(c, i):
                dve.wait_ge(direct0_ready, c + 1)
                nc.vector.tensor_reduce(y0[HALF:, bass.ds(c * BC, BC)],
                                        direct0[HALF:, i, :].rearrange("p (b d) -> p b d", d=D),
                                        mybir.AxisListType.X, ALU.add)

            def reduce1(c, i):
                dve.wait_ge(direct1_ready, c + 1)
                return nc.vector.tensor_reduce(y1[:, bass.ds(c * BC, BC)],
                                               direct1[:, i, :].rearrange("p (b d) -> p b d", d=D),
                                               mybir.AxisListType.X, ALU.add)

            def low(c, u, phase, k):
                layer, bank, tiles, mode = pairs(phase)[k]
                s, rows, nt = slot(u, phase, k), K0 if layer == 0 else K1, len(tiles)
                dve.wait_ge(hi_ready, done(c, phase, k + 1, (POOL, DVE)))
                nc.vector.tensor_tensor(prod_lo[:rows, s, :nt, :], prod[:rows, s, :nt, :],
                                        prod_hi[:rows, s, :nt, :].bitcast(f32), ALU.subtract).then_inc(dve_lo_ready, 1)

            def chunk(c, u, it, phase):
                owed = None
                for k, (layer, bank, tiles, mode) in enumerate(pairs(phase)):
                    s, rows, nt = slot(u, phase, k), K0 if layer == 0 else K1, len(tiles)
                    dve.wait_ge(bc_ready, done(c, phase, k + 1))
                    if layer == 0:
                        if tiles[0] == 0:
                            i = ring(u, 1)
                            dve.wait_ge(x_left_loaded[i], filling(u, it, 1) * 16)
                        i = ring(u, 1)
                        fixed, moving = x_left, bc0
                    else:
                        if tiles[0] == 0:
                            dve.wait_ge(h_ready, c + 1)
                        i = ring(u)
                        fixed, moving = h, bc1
                    if phase != "first" and not (isinstance(c, int) and c == 0 and 4 + k < SLOTS):
                        dve.wait_ge(pair_done, done(c, phase, k) - (SLOTS - 1))
                    other = fixed[:rows, i, :].unsqueeze(1).broadcast_to([rows, nt, NC])
                    nc.vector.tensor_tensor(prod[:rows, s, :nt, :], moving[:rows, bank:bank + nt, :], other,
                                            ALU.mult).then_inc(prod_ready, 1)
                    if owed is not None:
                        low(c, u, phase, owed)
                        owed = None
                    if mode == DVE:
                        owed = k
                    if phase != "first" and k == REDUCE_AT:
                        reduce0(c, ring(u))
                        if not (isinstance(c, int) and c == 0):
                            reduce1(c - 1, ring(u, -1))
                if owed is not None:
                    low(c, u, phase, owed)
                if phase == "first":
                    dve.wait_ge(w1_hi_ready, 1)
                    nc.vector.tensor_tensor(w_lo[:, T0:, :], w_in[:, T0:, :], w_hi[:, T0:, :].bitcast(f32),
                                            ALU.subtract).then_inc(w1_ready, 1)
                if phase == "last":
                    reduce1(c, ring(u)).then_inc(y_ready, 1)

            chunks(dve, chunk)

        @block.tensor
        def _(pe):
            def broadcast(c, u, phase, st):
                k = step_start(phase, st)
                layer = PHASES[phase][st][0][0]
                tiles = PHASES[phase][st][0][2]
                if layer == 0:
                    if tiles[0] == 0:
                        pe.wait_ge(x_half_ready, c + 2)
                    i = ring(u, 1)
                    if phase == "first":
                        if k:
                            pe.wait_ge(prod_ready, k)
                    else:
                        pe.wait_ge(prod_ready, prev_of_layer(c, phase, st, 0))
                    for e, t in enumerate(tiles):
                        last = nc.tensor.matmul(bc0[:K0, e, :], sel[:, t, :K0], x_half[:, i, :], start=True, stop=True)
                    last.then_inc(bc_ready, 1)
                else:
                    i = ring(u)
                    if not (isinstance(c, int) and c == 0 and tiles[0] == 0):
                        pe.wait_ge(prod_ready, prev_of_layer(c, phase, st, 1))
                    for g in range(GROUPS):
                        r = slice(32 * g, 32 * g + 32)
                        last = nc.tensor.matmul(bc1[:, g, :], sel[r, T0 + tiles[0], :], x_half[r, i, :],
                                                start=True, stop=True)
                        if g % 2:
                            last.then_inc(bc_ready, 1)

            def prev_of_layer(c, phase, st, layer):
                for p in range(st - 1, -1, -1):
                    if PHASES[phase][p][0][0] == layer:
                        return done(c, phase, step_start(phase, p) + len(PHASES[phase][p]))
                if isinstance(c, int) and c == 0:
                    return done(-1, "first", 4)
                for p in range(8, -1, -1):
                    if FULL[p][0][0] == layer:
                        return done(c - 1, "full", step_start("full", p) + len(FULL[p]))

            def contract(c, u, phase, st):
                k0 = step_start(phase, st)
                for k, (layer, bank, tiles, mode) in enumerate(PHASES[phase][st], k0):
                    s, rows = slot(u, phase, k), K0 if layer == 0 else K1
                    acc = acc1 if layer else acc0
                    first, final = tiles[0] == 0, tiles[-1] == (T0 if layer == 0 else T1) - 1
                    if first and layer == 0 and phase == "first":
                        pe.wait_ge(w0_ready, 1)
                    if first and layer == 1 and isinstance(c, int) and c == 0:
                        pe.wait_ge(w1_ready, 1)
                    if first and layer == 0 and phase != "first":
                        pe.wait_ge(direct0_ready, c + 1)
                    if first and layer == 1 and not (isinstance(c, int) and c == 0):
                        pe.wait_ge(direct1_ready, c)
                    at = 0 if layer == 0 else T0
                    if mode == NATIVE:
                        pe.wait_ge(prod_ready, done(c, phase, k + 1))
                        for e, t in enumerate(tiles):
                            last = nc.tensor.matmul(acc[:], weight(at + t), prod[:rows, s, e, :],
                                                    start=(first and e == 0), stop=(final and e == len(tiles) - 1))
                    else:
                        pe.wait_ge(hi_ready, done(c, phase, k + 1, (POOL, DVE)))
                        for e, t in enumerate(tiles):
                            nc.tensor.matmul(acc[:], w_hi[:rows, at + t, :], prod_hi[:rows, s, e, :],
                                             start=(first and e == 0), stop=False)
                            nc.tensor.matmul(acc[:], w_lo[:rows, at + t, :], prod_hi[:rows, s, e, :],
                                             start=False, stop=False)
                        if mode == POOL:
                            pe.wait_ge(lo_ready, done(c, phase, k + 1, (POOL,)))
                        else:
                            pe.wait_ge(dve_lo_ready, done(c, phase, k + 1, (DVE,)))
                        for e, t in enumerate(tiles):
                            last = nc.tensor.matmul(acc[:], w_hi[:rows, at + t, :], prod_lo[:rows, s, e, :],
                                                    start=False, stop=(final and e == len(tiles) - 1))
                    last.then_inc(pair_done, 1)

            pe.wait_ge(sel_ready, 1)
            for st in range(LAG):
                broadcast(-1, -2, "first", st)

            def chunk(c, u, it, phase):
                steps = PHASES[phase]
                for st in range(len(steps)):
                    ahead = st + LAG
                    if ahead < len(steps):
                        broadcast(c, u, phase, ahead)
                    elif phase != "last":
                        last_next = isinstance(c, int) and c + 1 == CHUNKS - 1
                        broadcast(c + 1, u + 1, "last" if last_next else "full", ahead - len(steps))
                    contract(c, u, phase, st)

            chunks(pe, chunk)


X_AT = 8
ACC1_AT = 3
REDUCE_AT = 6


def kernel(r_x, L0_rec_W0, L0_rec_b0, L0_rec_W1, L0_rec_b1):
    import concourse.bacc as bacc
    from concourse.bass_utils import run_bass_kernel_spmd

    f32 = mybir.dt.float32
    x = np.asarray(r_x)
    w0 = np.asarray(L0_rec_W0)
    w1 = np.asarray(L0_rec_W1)
    p, q = np.ogrid[:K0, :T0]
    i = p // ROT + 0 * q
    j = (i + ROT * q + p % ROT) % F
    sel, flags = sel_tables()
    arrays = {
        "x_dram": np.ascontiguousarray(x.transpose(1, 0, 2).reshape(F, N)),
        "w0_ij_dram": np.ascontiguousarray(w0[i, j]),
        "w0_ji_dram": np.ascontiguousarray(w0[j, i]),
        "w1_dram": np.ascontiguousarray(w1.reshape(T1, K1, S1).transpose(1, 0, 2)),
        "b0_dram": np.asarray(L0_rec_b0).reshape(S0, 1),
        "b1_dram": np.asarray(L0_rec_b1).reshape(S1, 1),
        "sel_dram": sel,
        "flags_dram": flags,
    }
    nc = bacc.Bacc("TRN2", target_bir_lowering=False, num_devices=1)
    d = {k: nc.dram_tensor(k, v.shape, f32, kind="ExternalInput").ap() for k, v in arrays.items()}
    y = nc.dram_tensor("y_dram", (S0 - HALF + S1, B), f32, kind="ExternalOutput").ap()
    build(nc, d["x_dram"], d["w0_ij_dram"], d["w0_ji_dram"], d["w1_dram"], d["b0_dram"],
          d["b1_dram"], d["sel_dram"], d["flags_dram"], y)
    r = run_bass_kernel_spmd(nc, [arrays], core_ids=[0])
    return np.ascontiguousarray(r.results[0]["y_dram"].T)
```

```python
from contextlib import ExitStack

import numpy as np

import concourse.bass as bass
from concourse import mybir

B, F, D = 512, 40, 32
S0, S1 = 128, 128
HALF = S0 // 2
N = B * D
NC = 512
CHUNKS = N // NC
BC = NC // D
XR = 2 * F
ROT = 128 // F
K0 = ROT * F
T0 = (F // 2 + 1) // ROT
K1 = 128
T1 = F * HALF // K1
T = T0 + T1

POOL, DVE, NATIVE = "pool", "dve", "native"
LAG = 5
RING = 3
BC_SLOTS, PROD_SLOTS, HI_SLOTS, LO_SLOTS = 3, 6, 14, 7


def _0(i, mode=DVE):
    return (0, tuple(t for t in (2 * i, 2 * i + 1) if t < T0), mode, 2 if i < 2 else 1)


def _1(i, mode=POOL):
    return (1, (2 * i, 2 * i + 1), mode, 0)


FULL = [_0(2), _1(0), _1(1), _0(3), _1(2, DVE), _1(3), _1(4), _1(5), _0(0), _1(6), _1(7), _0(1), _1(8), _1(9)]
PLACES = len(FULL)
START = [_0(i, NATIVE)[:3] + (1,) for i in range(4)] + [_0(0), _0(1)]
PHASES = {
    "first": [None] * (PLACES - len(START)) + START,
    "full": FULL,
    "late": [p if p[3] < 2 else None for p in FULL],
    "last": [p if p[3] < 1 else None for p in FULL],
}
PHASE_OF = {-1: "first", CHUNKS - 2: "late", CHUNKS - 1: "last"}
WAYS = (POOL, DVE, NATIVE)


def phase_of(c):
    return PHASE_OF.get(c, "full") if isinstance(c, int) else "full"


def counted(phase, k, ways):
    return sum(p is not None and p[2] in ways for p in PHASES[phase][:k])


def done(c, k=PLACES, ways=WAYS):
    if isinstance(c, int):
        return sum(counted(phase_of(b), PLACES, ways) for b in range(-1, c)) + counted(phase_of(c), k, ways)
    before = counted("first", PLACES, ways) + counted("full", k, ways)
    return counted("full", PLACES, ways) * c + before


def slot(u, k, slots):
    return ((1 + u) % RING * PLACES + k) % slots


def last_user(c, k, slots, ways):
    while True:
        k -= slots
        if k < 0:
            c, k = c - 1, k + PLACES
        if isinstance(c, int) and c < -1:
            return None
        pair = PHASES[phase_of(c)][k]
        if pair is not None and pair[2] in ways:
            return c, k, pair[2]


def rows_of(layer):
    return K1 if layer else K0


def sel_tables():
    sel = np.zeros((XR, T, 128), np.float32)
    for half in range(2):
        for t in range(T0):
            for p in range(K0):
                sel[2 * ((p // ROT + ROT * t + p % ROT) % F) + half, t, p] = 1
        for t in range(T1):
            for p in range(K1):
                sel[2 * (2 * t + p // HALF) + half, T0 + t, p] = 1
    p = np.arange(128)
    flags = np.stack([p % 2 == 1, p % ROT > 0, p % ROT < ROT - 1], 1).astype(np.float32)
    return sel, flags


def build(nc, xT, w0_ij, w0_ji, w1, sel_dram, columns_dram, yT):
    f32, f32r = mybir.dt.float32, mybir.dt.float32r
    ALU, ACT = mybir.AluOpType, mybir.ActivationFunctionType
    AX = mybir.AxisListType.X
    with ExitStack() as ctx:
        def sb(name, shape, dt=f32):
            return ctx.enter_context(nc.sbuf_tensor(name, shape, dt))

        def ps(name, shape):
            return ctx.enter_context(nc.psum_tensor(name, shape, f32))

        def sem(name):
            return ctx.enter_context(nc.semaphore(name))

        w = sb("w", [128, T, S0])
        w_hi = sb("w_hi", [128, T, S0], f32r)
        w_lo = sb("w_lo", [128, T, S0], f32r)
        sel = sb("sel", [XR, T, 128], f32r)
        columns = sb("columns", [128, 6])
        is_low, rotated, short = (columns[:, i:i + 1] for i in range(3))
        bias0, bias0h, bias1 = (columns[:, i:i + 1] for i in range(3, 6))
        x_rows = sb("x_rows", [XR, RING, NC])
        x_cut = sb("x_cut", [XR, NC], f32r)
        x_half = sb("x_half", [XR, RING, NC], f32r)
        x_left = sb("x_left", [128, RING, NC])
        outputs = sb("outputs", [128, 3, RING, NC])
        h = outputs[:, 0]
        direct0 = outputs[:, 1]
        direct1 = outputs[:, 2]
        prod = sb("prod", [128, PROD_SLOTS, 2, NC])
        prod_hi = sb("prod_hi", [128, HI_SLOTS, 2, NC], f32r)
        prod_lo = sb("prod_lo", [128, LO_SLOTS, 2, NC], f32r)
        y0 = sb("y0", [128, B])
        y1 = sb("y1", [128, B])
        flat = outputs[:].rearrange("p o i n -> p (o i n)")
        sel_in = flat[:XR, :T * 128].rearrange("p (t s) -> p t s", s=128)
        w0_back = flat[:, T * 128:(T + T0) * 128].rearrange("p (t s) -> p t s", s=S0)
        bc = ps("bc", [128, BC_SLOTS, 2, NC])
        acc0 = ps("acc0", [128, NC])
        acc1 = ps("acc1", [128, NC])

        columns_loaded, sel0_loaded, sel1_loaded = sem("columns_loaded"), sem("sel0_loaded"), sem("sel1_loaded")
        w0_loaded, w1_loaded = sem("w0_loaded"), sem("w1_loaded")
        x_rows_loaded = [sem(f"x_rows_loaded{i}") for i in range(RING)]
        x_left_loaded = [sem(f"x_left_loaded{i}") for i in range(RING)]
        sel_ready = sem("sel_ready")
        w0_summed = sem("w0_summed")
        w_hi_ready = sem("w_hi_ready")
        w_lo_ready = sem("w_lo_ready")
        x_cut_ready = sem("x_cut_ready")
        x_half_ready = sem("x_half_ready")
        bc_ready = sem("bc_ready")
        prod_ready = sem("prod_ready")
        hi_ready = sem("hi_ready")
        pool_lo_ready = sem("pool_lo_ready")
        dve_lo_ready = sem("dve_lo_ready")
        pair_done = sem("pair_done")
        h_ready = sem("h_ready")
        direct0_ready = sem("direct0_ready")
        direct1_ready = sem("direct1_ready")
        y_ready = sem("y_ready")
        y_stored = sem("y_stored")
        block = ctx.enter_context(nc.Block())

        def turns(engine, turn):
            turn(-1, -2, 0)
            turn(0, -1, 0)
            loops = (CHUNKS - 3) // RING
            with engine.Fori(0, loops) as it:
                for u in range(RING):
                    turn(it * RING + (1 + u), u, it)
            for c in range(1 + RING * loops, CHUNKS):
                turn(c, (c - 1) % RING, (c - 1) // RING)

        def ring(u, ahead=0):
            return (1 + u + ahead) % RING

        def filling(u, it, ahead):
            return it + ((1 + u + ahead) // RING + 1)

        def has_layer0(c):
            return not isinstance(c, int) or -1 <= c < CHUNKS - 1

        def layer0_end(c):
            return 1 + max(k for k, p in enumerate(PHASES[phase_of(c)])
                           if p is not None and p[0] == 0 and p[3] == 1)

        def at(c, place):
            return PLACES - 1 if isinstance(c, int) and c == -1 else place

        def has_before(c):
            return not isinstance(c, int) or c >= 1

        def makes_x(c):
            return not isinstance(c, int) or -1 <= c < CHUNKS - 3

        def wait_halves_free(engine, c, k, slots):
            user = last_user(c, k, slots, (POOL, DVE))
            if user is not None:
                engine.wait_ge(pair_done, done(user[0], user[1] + 1))

        @block.sync
        def _(sp):
            def load_chunk(c, i):
                x_of = xT[:, bass.ds(c * NC, NC)].unsqueeze(1)
                sp.dma_start(x_rows[:, i, :], x_of.broadcast_to([F, 2, NC])).then_inc(x_rows_loaded[i], 16)
                sp.dma_start(x_left[:K0, i, :], x_of.broadcast_to([F, ROT, NC])).then_inc(x_left_loaded[i], 16)

            sp.dma_start(columns[:], columns_dram).then_inc(columns_loaded, 16)
            load_chunk(0, 0)
            sp.dma_start(sel_in[:, :T0, :], sel_dram[:, :T0, :]).then_inc(sel0_loaded, 16)
            load_chunk(1, 1)
            sp.dma_start(sel_in[:, T0:, :], sel_dram[:, T0:, :]).then_inc(sel1_loaded, 16)
            load_chunk(2, 2)

            def refill(c, i):
                sp.wait_ge(x_half_ready, c - (RING - 1))
                sp.wait_ge(prod_ready, done(c - (RING + 1)))
                load_chunk(c, i)

            loops = (CHUNKS - RING - 1) // RING
            refill(RING, 0)
            with sp.Fori(0, loops) as it:
                for u in range(RING):
                    refill(it * RING + (RING + 1 + u), (1 + u) % RING)
            for c in range(RING + 1 + RING * loops, CHUNKS):
                refill(c, c % RING)
            sp.wait_ge(y_ready, 1)
            sp.dma_start(yT[:HALF, :], y0[HALF:, :]).then_inc(y_stored, 16)
            sp.dma_start(yT[HALF:, :], y1[:]).then_inc(y_stored, 16)
            sp.wait_ge(y_stored, 32)

        @block.gpsimd
        def _(pool):
            def halve(c, i):
                pool.wait_ge(x_cut_ready, c + 1)
                nc.gpsimd.tensor_tensor(x_half[:, i, :], x_rows[:, i, :], x_cut[:].bitcast(f32),
                                        ALU.subtract).then_inc(x_half_ready, 1)

            halve(0, 0)
            pool.wait_ge(w_hi_ready, 1)
            nc.gpsimd.tensor_tensor(w_lo[:K0, :T0, :], w[:K0, :T0, :], w_hi[:K0, :T0, :].bitcast(f32),
                                    ALU.subtract).then_inc(w_lo_ready, 1)
            halve(1, 1)
            pool.wait_ge(w_hi_ready, 2)
            nc.gpsimd.tensor_tensor(w_lo[:, T0:, :], w[:, T0:, :], w_hi[:, T0:, :].bitcast(f32),
                                    ALU.subtract).then_inc(w_lo_ready, 1)

            def turn(c, u, it):
                for k, pair in enumerate(PHASES[phase_of(c)]):
                    if pair is not None and pair[2] == POOL:
                        p, hi, lo = slot(u, k, PROD_SLOTS), slot(u, k, HI_SLOTS), slot(u, k, LO_SLOTS)
                        pool.wait_ge(hi_ready, done(c, k + 1, (POOL, DVE)))
                        wait_halves_free(pool, c, k, LO_SLOTS)
                        nc.gpsimd.tensor_tensor(prod_lo[:, lo], prod[:, p], prod_hi[:, hi].bitcast(f32),
                                                ALU.subtract).then_inc(pool_lo_ready, 1)
                    if k == X_AT and makes_x(c):
                        if has_before(c) or c == 0:
                            pool.wait_ge(bc_ready, done(c))
                        halve(c + 3, ring(u, 3))

            turns(pool, turn)

        @block.scalar
        def _(act):
            act.dma_start(w[:K0, :T0, :], w0_ij).then_inc(w0_loaded, 16)
            act.dma_start(w0_back[:K0], w0_ji).then_inc(w0_loaded, 16)
            act.dma_start(w[:, T0:, :], w1).then_inc(w1_loaded, 16)

            def cut(c, i, times):
                act.wait_ge(x_rows_loaded[i], times * 16)
                if not isinstance(c, int) or c > 0:
                    act.wait_ge(x_half_ready, c)
                nc.scalar.activation(x_cut[:], x_rows[:, i, :], ACT.Copy, scale=is_low[:XR]).then_inc(x_cut_ready, 1)

            act.wait_ge(columns_loaded, 16)
            cut(0, 0, 1)
            act.wait_ge(sel0_loaded, 16)
            nc.scalar.copy(sel[:, :T0, :], sel_in[:, :T0, :]).then_inc(sel_ready, 1)
            act.wait_ge(w0_summed, 1)
            nc.scalar.copy(w_hi[:K0, :T0, :], w[:K0, :T0, :]).then_inc(w_hi_ready, 1)
            cut(1, 1, 1)
            act.wait_ge(sel1_loaded, 16)
            nc.scalar.copy(sel[:, T0:, :], sel_in[:, T0:, :]).then_inc(sel_ready, 1)
            act.wait_ge(w1_loaded, 16)
            nc.scalar.copy(w_hi[:, T0:, :], w[:, T0:, :]).then_inc(w_hi_ready, 1)

            def read_acc0(c, i, pairs):
                act.wait_ge(pair_done, pairs)
                nc.scalar.activation(h[:HALF, i, :], acc0[:HALF, :], ACT.Relu, bias=bias0h[:HALF])
                nc.scalar.activation(h[HALF:, i, :], acc0[:HALF, :], ACT.Relu, bias=bias0h[HALF:]).then_inc(h_ready, 1)
                nc.scalar.activation(direct0[HALF:, i, :], acc0[HALF:, :], ACT.Relu, bias=bias0[HALF:]).then_inc(direct0_ready, 1)

            def read_acc1(c, i):
                act.wait_ge(pair_done, done(c))
                nc.scalar.activation(direct1[:, i, :], acc1[:], ACT.Relu, bias=bias1).then_inc(direct1_ready, 1)

            def turn(c, u, it):
                for k, pair in enumerate(PHASES[phase_of(c)]):
                    if pair is not None and pair[2] != NATIVE:
                        layer, tiles, mode, ahead = pair
                        rows, nt, hi = rows_of(layer), len(tiles), slot(u, k, HI_SLOTS)
                        act.wait_ge(prod_ready, done(c, k + 1))
                        wait_halves_free(act, c, k, HI_SLOTS)
                        of = bc[:rows, slot(u, k, BC_SLOTS), :nt, :] if mode == DVE else prod[:rows, slot(u, k, PROD_SLOTS), :nt, :]
                        nc.scalar.copy(prod_hi[:rows, hi, :nt, :], of).then_inc(hi_ready, 1)
                    if k == ACC1_AT and has_before(c):
                        read_acc1(c - 1, ring(u, -1))
                    if k == at(c, ACC0_AT) and has_layer0(c):
                        read_acc0(c + 1, ring(u, 1), done(c, layer0_end(c)))
                    if k == X_AT and makes_x(c):
                        cut(c + 3, ring(u, 3), filling(u, it, 3))
                if isinstance(c, int) and c == CHUNKS - 1:
                    read_acc1(c, ring(u))

            turns(act, turn)

        @block.vector
        def _(dve):
            dve.wait_ge(w0_loaded, 32)
            dve.wait_ge(columns_loaded, 16)
            for t, flag in ((0, rotated), (T0 - 1, short)):
                nc.vector.scalar_tensor_tensor(w[:K0, t, :], w0_back[:K0, t, :], flag[:K0],
                                               w[:K0, t, :], ALU.mult, ALU.add)
            nc.vector.tensor_tensor(w[:K0, 1:T0 - 1, :], w[:K0, 1:T0 - 1, :], w0_back[:K0, 1:T0 - 1, :],
                                    ALU.add).then_inc(w0_summed, 1)
            dve.wait_ge(w0_summed, 1)

            def reduce0(c, i):
                dve.wait_ge(direct0_ready, c + 1)
                nc.vector.tensor_reduce(y0[HALF:, bass.ds(c * BC, BC)],
                                        direct0[HALF:, i, :].rearrange("p (b d) -> p b d", d=D), AX, ALU.add)

            def reduce1(c, i):
                dve.wait_ge(direct1_ready, c + 1)
                return nc.vector.tensor_reduce(y1[:, bass.ds(c * BC, BC)],
                                               direct1[:, i, :].rearrange("p (b d) -> p b d", d=D), AX, ALU.add)

            def low(c, u, k, layer, tiles):
                rows, nt, hi, lo = rows_of(layer), len(tiles), slot(u, k, HI_SLOTS), slot(u, k, LO_SLOTS)
                dve.wait_ge(hi_ready, done(c, k + 1, (POOL, DVE)))
                wait_halves_free(dve, c, k, LO_SLOTS)
                nc.vector.tensor_tensor(prod_lo[:rows, lo, :nt, :], bc[:rows, slot(u, k, BC_SLOTS), :nt, :],
                                        prod_hi[:rows, hi, :nt, :].bitcast(f32), ALU.subtract).then_inc(dve_lo_ready, 1)

            def turn(c, u, it):
                places = PHASES[phase_of(c)]
                owed = None
                for k, pair in enumerate(places):
                    if pair is not None:
                        layer, tiles, mode, ahead = pair
                        rows, nt, i = rows_of(layer), len(tiles), ring(u, ahead)
                        b, p = slot(u, k, BC_SLOTS), slot(u, k, PROD_SLOTS)
                        dve.wait_ge(bc_ready, done(c, k + 1))
                        if layer == 0 and tiles[0] == 0:
                            dve.wait_ge(x_left_loaded[i], filling(u, it, ahead) * 16)
                        if layer == 1 and tiles[0] == 0:
                            dve.wait_ge(h_ready, c + 1)
                        if mode != DVE:
                            user = last_user(c, k, PROD_SLOTS, (POOL, NATIVE))
                            if user is not None and user[2] == POOL:
                                dve.wait_ge(pool_lo_ready, done(user[0], user[1] + 1, (POOL,)))
                            elif user is not None:
                                dve.wait_ge(pair_done, done(user[0], user[1] + 1))
                        fixed = (h if layer else x_left)[:rows, i, :].unsqueeze(1).broadcast_to([rows, nt, NC])
                        to = bc[:rows, b, :nt, :] if mode == DVE else prod[:rows, p, :nt, :]
                        nc.vector.tensor_tensor(to, bc[:rows, b, :nt, :], fixed, ALU.mult).then_inc(prod_ready, 1)
                    if owed is not None:
                        low(c, u, owed, *places[owed][:2])
                    owed = k if pair is not None and pair[2] == DVE else None
                    if owed is not None and (k + 1 == PLACES or places[k + 1] is None):
                        low(c, u, owed, *places[owed][:2])
                        owed = None
                    if k == at(c, REDUCE0_AT) and has_layer0(c):
                        reduce0(c + 1, ring(u, 1))
                    if k == REDUCE1_AT and has_before(c):
                        reduce1(c - 1, ring(u, -1))
                if isinstance(c, int) and c == CHUNKS - 1:
                    reduce1(c, ring(u)).then_inc(y_ready, 1)

            turns(dve, turn)

        @block.tensor
        def _(pe):
            def broadcast(c, u, k):
                pair = PHASES[phase_of(c)][k]
                if pair is None:
                    return
                layer, tiles, mode, ahead = pair
                i, b = ring(u, ahead), slot(u, k, BC_SLOTS)
                if layer == 0 and tiles[0] == 0:
                    pe.wait_ge(x_half_ready, c + ahead + 1)
                if isinstance(c, int) and c == 0 and layer == 1 and tiles[0] == 0:
                    pe.wait_ge(sel_ready, 2)
                user = last_user(c, k, BC_SLOTS, WAYS)
                if user is not None and user[2] == DVE:
                    pe.wait_ge(dve_lo_ready, done(user[0], user[1] + 1, (DVE,)))
                elif user is not None:
                    pe.wait_ge(prod_ready, done(user[0], user[1] + 1))
                for e, t in enumerate(tiles):
                    last = nc.tensor.matmul(bc[:rows_of(layer), b, e, :], sel[:, layer * T0 + t, :rows_of(layer)],
                                            x_half[:, i, :], start=True, stop=True)
                last.then_inc(bc_ready, 1)

            def contract(c, u, k):
                pair = PHASES[phase_of(c)][k]
                if pair is None:
                    return
                layer, tiles, mode, ahead = pair
                rows, acc = rows_of(layer), acc1 if layer else acc0
                p, hi, lo = slot(u, k, PROD_SLOTS), slot(u, k, HI_SLOTS), slot(u, k, LO_SLOTS)
                first, final = tiles[0] == 0, tiles[-1] == (T1 if layer else T0) - 1
                if first and layer == 0:
                    if isinstance(c, int) and c + ahead == 0:
                        pe.wait_ge(w0_summed, 1)
                    else:
                        pe.wait_ge(direct0_ready, c + ahead)
                    if isinstance(c, int) and c + ahead == 1:
                        pe.wait_ge(w_lo_ready, 1)
                if first and layer == 1:
                    if isinstance(c, int) and c == 0:
                        pe.wait_ge(w_lo_ready, 2)
                    else:
                        pe.wait_ge(direct1_ready, c)
                if mode == NATIVE:
                    pe.wait_ge(prod_ready, done(c, k + 1))
                    for e, t in enumerate(tiles):
                        last = nc.tensor.matmul(acc[:], w[:rows, layer * T0 + t, :], prod[:rows, p, e, :],
                                                start=(first and e == 0), stop=(final and e == len(tiles) - 1))
                else:
                    pe.wait_ge(hi_ready, done(c, k + 1, (POOL, DVE)))
                    for e, t in enumerate(tiles):
                        nc.tensor.matmul(acc[:], w_hi[:rows, layer * T0 + t, :], prod_hi[:rows, hi, e, :],
                                         start=(first and e == 0), stop=False)
                        nc.tensor.matmul(acc[:], w_lo[:rows, layer * T0 + t, :], prod_hi[:rows, hi, e, :],
                                         start=False, stop=False)
                    lo_ready = pool_lo_ready if mode == POOL else dve_lo_ready
                    pe.wait_ge(lo_ready, done(c, k + 1, (mode,)))
                    for e, t in enumerate(tiles):
                        last = nc.tensor.matmul(acc[:], w_hi[:rows, layer * T0 + t, :], prod_lo[:rows, lo, e, :],
                                                start=False, stop=(final and e == len(tiles) - 1))
                last.then_inc(pair_done, 1)

            pe.wait_ge(sel_ready, 1)

            def turn(c, u, it):
                start = PLACES - len(START) if isinstance(c, int) and c == -1 else 0
                for k in range(start, start + LAG if start else 0):
                    broadcast(c, u, k)
                for k in range(start, PLACES):
                    if k + LAG < PLACES:
                        broadcast(c, u, k + LAG)
                    elif not isinstance(c, int) or c < CHUNKS - 1:
                        broadcast(c + 1, u + 1, k + LAG - PLACES)
                    contract(c, u, k)

            turns(pe, turn)


ACC1_AT = 3
ACC0_AT = 8
REDUCE1_AT = 6
REDUCE0_AT = 10
X_AT = 11


def kernel(r_x, L0_rec_W0, L0_rec_b0, L0_rec_W1, L0_rec_b1):
    import concourse.bacc as bacc
    from concourse.bass_utils import run_bass_kernel_spmd

    f32 = mybir.dt.float32
    x, w0, w1 = np.asarray(r_x), np.asarray(L0_rec_W0), np.asarray(L0_rec_W1)
    p, q = np.ogrid[:K0, :T0]
    i = p // ROT + 0 * q
    j = (i + ROT * q + p % ROT) % F
    sel, flags = sel_tables()
    b0, b1 = np.asarray(L0_rec_b0), np.asarray(L0_rec_b1)
    arrays = {
        "x_dram": np.ascontiguousarray(x.transpose(1, 0, 2).reshape(F, N)),
        "w0_ij_dram": np.ascontiguousarray(w0[i, j]),
        "w0_ji_dram": np.ascontiguousarray(w0[j, i]),
        "w1_dram": np.ascontiguousarray(w1.reshape(T1, K1, S1).transpose(1, 0, 2)),
        "sel_dram": sel,
        "columns_dram": np.concatenate([flags, np.stack([b0, np.tile(b0[:HALF], 2), b1], 1)], 1),
    }
    nc = bacc.Bacc("TRN2", target_bir_lowering=False, num_devices=1)
    d = {k: nc.dram_tensor(k, v.shape, f32, kind="ExternalInput").ap() for k, v in arrays.items()}
    y = nc.dram_tensor("y_dram", (S0 - HALF + S1, B), f32, kind="ExternalOutput").ap()
    build(nc, d["x_dram"], d["w0_ij_dram"], d["w0_ji_dram"], d["w1_dram"], d["sel_dram"],
          d["columns_dram"], y)
    r = run_bass_kernel_spmd(nc, [arrays], core_ids=[0])
    return np.ascontiguousarray(r.results[0]["y_dram"].T)
```

```python
from contextlib import ExitStack

import numpy as np

import concourse.bass as bass
from concourse import mybir

B, F, D = 512, 40, 32
S0, S1 = 128, 128
HALF = S0 // 2
N = B * D
NC = 512
CHUNKS = N // NC
BC = NC // D
XR = 2 * F
ROT = 128 // F
K0 = ROT * F
T0 = (F // 2 + 1) // ROT
K1 = 128
T1 = F * HALF // K1
T = T0 + T1
PAIRS0 = (T0 + 1) // 2

POOL, DVE, NATIVE = "pool", "dve", "native"
LAG = 5
START_LAG = 4
ACC1_AT, ACC0_AT, FIRST_ACC0_AT = 3, 8, 0
REDUCE1_AT, REDUCE0_AT, FIRST_REDUCE0_AT = 6, 12, 2
X_AT = 11
RING = 3
ROT_SLOTS = 6
BC_SLOTS, PROD_SLOTS, HI_SLOTS, LO_SLOTS = 3, 6, 6, 6


def tiles_of(layer, i):
    return tuple(t for t in (2 * i, 2 * i + 1) if t < (T1 if layer else T0))


def _0(i, mode=DVE):
    return (0, tiles_of(0, i), mode, 2 if i < 2 else 1)


def _1(i, mode=POOL):
    return (1, tiles_of(1, i), mode, 0)


FULL = [_0(2), _1(0), _1(1), _0(3), _1(2, DVE), _1(3), _1(4), _1(5), _0(0), _1(6), _1(7), _0(1), _1(8), _1(9)]
PLACES = len(FULL)
START = [_0(i, NATIVE)[:3] + (1,) for i in range(PAIRS0)] + [_0(0, POOL), _0(1, POOL)]
LAST = [_1(0), _1(1), _1(2, DVE), _1(3), _1(4, DVE), _1(5), _1(6, DVE), _1(7), _1(8), _1(9, DVE)]
PHASES = {
    "first": [None] * (PLACES - len(START)) + START,
    "full": FULL,
    "late": [p if p[3] < 2 else None for p in FULL],
    "last": LAST + [None] * (PLACES - len(LAST)),
}
PHASE_OF = {-1: "first", CHUNKS - 2: "late", CHUNKS - 1: "last"}
WAYS = (POOL, DVE, NATIVE)


def phase_of(c):
    return PHASE_OF.get(c, "full") if isinstance(c, int) else "full"


def counted(phase, k, ways):
    return sum(p is not None and p[2] in ways for p in PHASES[phase][:k])


def done(c, k=PLACES, ways=WAYS):
    if isinstance(c, int):
        return sum(counted(phase_of(b), PLACES, ways) for b in range(-1, c)) + counted(phase_of(c), k, ways)
    before = counted("first", PLACES, ways) + counted("full", k, ways)
    return counted("full", PLACES, ways) * c + before


def slot(u, k, slots):
    return ((1 + u) % RING * PLACES + k) % slots


def last_user(c, k, slots, ways):
    while True:
        k -= slots
        if k < 0:
            c, k = c - 1, k + PLACES
        if isinstance(c, int) and c < -1:
            return None
        pair = PHASES[phase_of(c)][k]
        if pair is not None and pair[2] in ways:
            return c, k, pair[2]


def place_of(c, i):
    if isinstance(c, int) and (c == 0 or c == 1 and i < 2):
        return -1, PLACES - len(START) + c * PAIRS0 + i
    return next((c - p[3], k) for k, p in enumerate(FULL) if p[0] == 0 and p[1][0] == 2 * i)


def rot_slot(c, i):
    return (PAIRS0 * c + i) % ROT_SLOTS


def rows_of(layer):
    return K1 if layer else K0


def sel_tables():
    sel = np.zeros((XR, 1 + T1, 128), np.float32)
    for half in range(2):
        for p in range(K0):
            sel[2 * (p // ROT) + half, 0, p] = 1
        for t in range(T1):
            for p in range(K1):
                sel[2 * (2 * t + p // HALF) + half, 1 + t, p] = 1
    p = np.arange(128)
    flags = np.stack([p % 2 == 1, p % ROT > 0, p % ROT < ROT - 1], 1).astype(np.float32)
    return sel, flags


def build(nc, xT, w0_ij, w0_ji, w1, sel_dram, columns_dram, yT):
    f32, f32r = mybir.dt.float32, mybir.dt.float32r
    ALU, ACT = mybir.AluOpType, mybir.ActivationFunctionType
    AX = mybir.AxisListType.X
    with ExitStack() as ctx:
        def sb(name, shape, dt=f32):
            return ctx.enter_context(nc.sbuf_tensor(name, shape, dt))

        def ps(name, shape):
            return ctx.enter_context(nc.psum_tensor(name, shape, f32))

        def sem(name):
            return ctx.enter_context(nc.semaphore(name))

        w = sb("w", [128, T, S0])
        w_hi = sb("w_hi", [128, T, S0], f32r)
        w_lo = sb("w_lo", [128, T, S0], f32r)
        sel = sb("sel", [XR, 1 + T1, 128], f32r)
        columns = sb("columns", [128, 6])
        is_low, rotated, short = (columns[:, i:i + 1] for i in range(3))
        bias0, bias0h, bias1 = (columns[:, i:i + 1] for i in range(3, 6))
        x_rows = sb("x_rows", [XR, RING, NC])
        x_cut = sb("x_cut", [XR, NC], f32r)
        x_half = sb("x_half", [XR, RING, NC], f32r)
        x_rot = sb("x_rot", [128, ROT_SLOTS, 2, NC])
        outputs = sb("outputs", [128, 3, RING, NC])
        h = outputs[:, 0]
        direct0 = outputs[:, 1]
        direct1 = outputs[:, 2]
        prod = sb("prod", [128, PROD_SLOTS, 2, NC])
        prod_hi = sb("prod_hi", [128, HI_SLOTS, 2, NC], f32r)
        prod_lo = sb("prod_lo", [128, LO_SLOTS, 2, NC], f32r)
        y0 = sb("y0", [128, B])
        y1 = sb("y1", [128, B])
        flat = outputs[:].rearrange("p o i n -> p (o i n)")
        sel_in = flat[:XR, :(1 + T1) * 128].rearrange("p (t s) -> p t s", s=128)
        w0_back = flat[:, (1 + T1) * 128:(1 + T1 + T0) * 128].rearrange("p (t s) -> p t s", s=S0)
        bc = ps("bc", [128, BC_SLOTS, 2, NC])
        acc0 = ps("acc0", [128, NC])
        acc1 = ps("acc1", [128, NC])

        columns_loaded, sel0_loaded, sel1_loaded = sem("columns_loaded"), sem("sel0_loaded"), sem("sel1_loaded")
        w0_loaded, w1_loaded = sem("w0_loaded"), sem("w1_loaded")
        x_rows_loaded = [sem(f"x_rows_loaded{i}") for i in range(RING)]
        x_rot_loaded = [[sem(f"x_rot_loaded{r}_{i}") for i in range(PAIRS0)] for r in range(RING)]
        sel_ready = sem("sel_ready")
        w0_summed = sem("w0_summed")
        w_hi_ready = sem("w_hi_ready")
        w_lo_ready = sem("w_lo_ready")
        x_cut_ready = sem("x_cut_ready")
        x_half_ready = sem("x_half_ready")
        bc_ready = sem("bc_ready")
        prod_ready = sem("prod_ready")
        hi_ready = sem("hi_ready")
        pool_lo_ready = sem("pool_lo_ready")
        dve_lo_ready = sem("dve_lo_ready")
        pair_done = sem("pair_done")
        h_ready = sem("h_ready")
        direct0_ready = sem("direct0_ready")
        direct1_ready = sem("direct1_ready")
        y0_ready, y1_ready = sem("y0_ready"), sem("y1_ready")
        y_stored = sem("y_stored")
        block = ctx.enter_context(nc.Block())

        def turns(engine, turn):
            turn(-1, -2, 0)
            turn(0, -1, 0)
            loops = (CHUNKS - 3) // RING
            with engine.Fori(0, loops) as it:
                for u in range(RING):
                    turn(it * RING + (1 + u), u, it)
            for c in range(1 + RING * loops, CHUNKS):
                turn(c, (c - 1) % RING, (c - 1) // RING)

        def ring(u, ahead=0):
            return (1 + u + ahead) % RING

        def filling(u, it, ahead):
            return it + ((1 + u + ahead) // RING + 1)

        def has_layer0(c):
            return not isinstance(c, int) or -1 <= c < CHUNKS - 1

        def layer0_end(c):
            return 1 + max(k for k, p in enumerate(PHASES[phase_of(c)])
                           if p is not None and p[0] == 0 and p[3] == 1)

        def starts(c):
            return isinstance(c, int) and c == -1

        def has_before(c):
            return not isinstance(c, int) or c >= 1

        def makes_x(c):
            return not isinstance(c, int) or -1 <= c < CHUNKS - 3

        def wait_halves_free(engine, c, k, slots):
            user = last_user(c, k, slots, (POOL, DVE))
            if user is not None:
                engine.wait_ge(pair_done, done(user[0], user[1] + 1))

        @block.sync
        def _(sp):
            def load_rows(c, i):
                x_of = xT[:F, bass.ds(c * NC, NC)].unsqueeze(1)
                sp.dma_start(x_rows[:, i, :], x_of.broadcast_to([F, 2, NC])).then_inc(x_rows_loaded[i], 16)

            def load_rot(c, u, i):
                s, r = rot_slot(1 + u, i), (1 + u) % RING
                for e, t in enumerate(tiles_of(0, i)):
                    first = xT[ROT * t:ROT * t + F, bass.ds(c * NC, NC)]
                    x_of = bass.AP(first.tensor, first.offset, [[N, F], [N, ROT], [1, NC]])
                    sp.dma_start(x_rot[:K0, s, e, :], x_of).then_inc(x_rot_loaded[r][i], 16)

            def reload_rot(c, u, i):
                behind = PAIRS0 + i - ROT_SLOTS
                turn, k = place_of(c - 1, behind) if behind >= 0 else place_of(c - 2, behind + PAIRS0)
                sp.wait_ge(prod_ready, done(turn, k + 1))
                load_rot(c, u, i)

            sp.dma_start(columns[:], columns_dram).then_inc(columns_loaded, 16)
            load_rows(0, 0)
            sp.dma_start(sel_in[:, :1, :], sel_dram[:, :1, :]).then_inc(sel0_loaded, 16)
            load_rot(0, -1, 0)
            load_rows(1, 1)
            for i in range(1, PAIRS0):
                load_rot(0, -1, i)
            sp.dma_start(sel_in[:, 1:, :], sel_dram[:, 1:, :]).then_inc(sel1_loaded, 16)
            load_rot(1, 0, 0)
            load_rot(1, 0, 1)
            load_rows(2, 2)
            reload_rot(1, 0, 2)
            reload_rot(1, 0, 3)
            for i in range(PAIRS0):
                reload_rot(2, 1, i)

            def refill(c, u):
                sp.wait_ge(x_half_ready, c - (RING - 1))
                load_rows(c, (1 + u) % RING)
                for i in range(PAIRS0):
                    reload_rot(c, u, i)

            loops = (CHUNKS - RING - 1) // RING
            refill(RING, -1)
            with sp.Fori(0, loops) as it:
                for u in range(RING):
                    refill(it * RING + (RING + 1 + u), u)
            for c in range(RING + 1 + RING * loops, CHUNKS):
                refill(c, (c - 1) % RING)
            sp.wait_ge(y0_ready, 1)
            sp.dma_start(yT[:HALF, :], y0[HALF:, :]).then_inc(y_stored, 16)
            sp.wait_ge(y1_ready, 1)
            sp.dma_start(yT[HALF:, :], y1[:]).then_inc(y_stored, 16)
            sp.wait_ge(y_stored, 32)

        @block.gpsimd
        def _(pool):
            def halve(c, i):
                pool.wait_ge(x_cut_ready, c + 1)
                nc.gpsimd.tensor_tensor(x_half[:, i, :], x_rows[:, i, :], x_cut[:].bitcast(f32),
                                        ALU.subtract).then_inc(x_half_ready, 1)

            halve(0, 0)
            pool.wait_ge(w_hi_ready, 1)
            nc.gpsimd.tensor_tensor(w_lo[:K0, :T0, :], w[:K0, :T0, :], w_hi[:K0, :T0, :].bitcast(f32),
                                    ALU.subtract).then_inc(w_lo_ready, 1)
            halve(1, 1)
            pool.wait_ge(w_hi_ready, 2)
            nc.gpsimd.tensor_tensor(w_lo[:, T0:, :], w[:, T0:, :], w_hi[:, T0:, :].bitcast(f32),
                                    ALU.subtract).then_inc(w_lo_ready, 1)

            def turn(c, u, it):
                for k, pair in enumerate(PHASES[phase_of(c)]):
                    if pair is not None and pair[2] == POOL:
                        p, hi, lo = slot(u, k, PROD_SLOTS), slot(u, k, HI_SLOTS), slot(u, k, LO_SLOTS)
                        pool.wait_ge(hi_ready, done(c, k + 1, (POOL, DVE)))
                        wait_halves_free(pool, c, k, LO_SLOTS)
                        rows, nt = rows_of(pair[0]), len(pair[1])
                        nc.gpsimd.tensor_tensor(prod_lo[:rows, lo, :nt], prod[:rows, p, :nt],
                                                prod_hi[:rows, hi, :nt].bitcast(f32),
                                                ALU.subtract).then_inc(pool_lo_ready, 1)
                    if k == X_AT and makes_x(c):
                        if has_before(c) or c == 0:
                            pool.wait_ge(bc_ready, done(c))
                        halve(c + 3, ring(u, 3))

            turns(pool, turn)

        @block.scalar
        def _(act):
            act.dma_start(w[:K0, :T0, :], w0_ij).then_inc(w0_loaded, 16)
            act.dma_start(w0_back[:K0], w0_ji).then_inc(w0_loaded, 16)
            act.dma_start(w[:, T0:, :], w1).then_inc(w1_loaded, 16)

            def cut(c, i, times):
                act.wait_ge(x_rows_loaded[i], times * 16)
                if not isinstance(c, int) or c > 0:
                    act.wait_ge(x_half_ready, c)
                nc.scalar.activation(x_cut[:], x_rows[:, i, :], ACT.Copy, scale=is_low[:XR]).then_inc(x_cut_ready, 1)

            act.wait_ge(columns_loaded, 16)
            cut(0, 0, 1)
            act.wait_ge(sel0_loaded, 16)
            nc.scalar.copy(sel[:, :1, :], sel_in[:, :1, :]).then_inc(sel_ready, 1)
            act.wait_ge(w0_summed, 1)
            nc.scalar.copy(w_hi[:K0, :T0, :], w[:K0, :T0, :]).then_inc(w_hi_ready, 1)
            cut(1, 1, 1)
            act.wait_ge(w1_loaded, 16)
            nc.scalar.copy(w_hi[:, T0:, :], w[:, T0:, :]).then_inc(w_hi_ready, 1)
            act.wait_ge(sel1_loaded, 16)
            nc.scalar.copy(sel[:, 1:, :], sel_in[:, 1:, :]).then_inc(sel_ready, 1)

            def read_acc0(c, i, pairs):
                act.wait_ge(pair_done, pairs)
                nc.scalar.activation(h[:HALF, i, :], acc0[:HALF, :], ACT.Relu, bias=bias0h[:HALF])
                nc.scalar.activation(h[HALF:, i, :], acc0[:HALF, :], ACT.Relu,
                                     bias=bias0h[HALF:]).then_inc(h_ready, 1)
                nc.scalar.activation(direct0[HALF:, i, :], acc0[HALF:, :], ACT.Relu,
                                     bias=bias0[HALF:]).then_inc(direct0_ready, 1)

            def read_acc1(c, i):
                act.wait_ge(pair_done, done(c))
                nc.scalar.activation(direct1[:, i, :], acc1[:], ACT.Relu, bias=bias1).then_inc(direct1_ready, 1)

            def turn(c, u, it):
                for k, pair in enumerate(PHASES[phase_of(c)]):
                    if pair is not None and pair[2] != NATIVE:
                        layer, tiles, mode, ahead = pair
                        rows, nt, hi = rows_of(layer), len(tiles), slot(u, k, HI_SLOTS)
                        act.wait_ge(prod_ready, done(c, k + 1))
                        wait_halves_free(act, c, k, HI_SLOTS)
                        of = bc[:, slot(u, k, BC_SLOTS)] if mode == DVE else prod[:, slot(u, k, PROD_SLOTS)]
                        nc.scalar.copy(prod_hi[:rows, hi, :nt, :], of[:rows, :nt, :]).then_inc(hi_ready, 1)
                    if k == ACC1_AT and has_before(c):
                        read_acc1(c - 1, ring(u, -1))
                    if k == FIRST_ACC0_AT and isinstance(c, int) and c == 0:
                        read_acc0(0, 0, done(-1, layer0_end(-1)))
                    if k == ACC0_AT and has_layer0(c) and not starts(c):
                        read_acc0(c + 1, ring(u, 1), done(c, layer0_end(c)))
                    if k == X_AT and makes_x(c):
                        cut(c + 3, ring(u, 3), filling(u, it, 3))
                if isinstance(c, int) and c == CHUNKS - 1:
                    read_acc1(c, ring(u))

            turns(act, turn)

        @block.vector
        def _(dve):
            dve.wait_ge(w0_loaded, 32)
            dve.wait_ge(columns_loaded, 16)
            for t, flag in ((0, rotated), (T0 - 1, short)):
                nc.vector.scalar_tensor_tensor(w[:K0, t, :], w0_back[:K0, t, :], flag[:K0],
                                               w[:K0, t, :], ALU.mult, ALU.add)
            nc.vector.tensor_tensor(w[:K0, 1:T0 - 1, :], w[:K0, 1:T0 - 1, :], w0_back[:K0, 1:T0 - 1, :],
                                    ALU.add).then_inc(w0_summed, 1)
            dve.wait_ge(w0_summed, 1)

            def reduce0(c, i):
                dve.wait_ge(direct0_ready, c + 1)
                return nc.vector.tensor_reduce(y0[HALF:, bass.ds(c * BC, BC)],
                                        direct0[HALF:, i, :].rearrange("p (b d) -> p b d", d=D), AX, ALU.add)

            def reduce1(c, i):
                dve.wait_ge(direct1_ready, c + 1)
                return nc.vector.tensor_reduce(y1[:, bass.ds(c * BC, BC)],
                                               direct1[:, i, :].rearrange("p (b d) -> p b d", d=D), AX, ALU.add)

            def low(c, u, k, layer, tiles):
                rows, nt, hi, lo = rows_of(layer), len(tiles), slot(u, k, HI_SLOTS), slot(u, k, LO_SLOTS)
                dve.wait_ge(hi_ready, done(c, k + 1, (POOL, DVE)))
                wait_halves_free(dve, c, k, LO_SLOTS)
                nc.vector.tensor_tensor(prod_lo[:rows, lo, :nt, :], bc[:rows, slot(u, k, BC_SLOTS), :nt, :],
                                        prod_hi[:rows, hi, :nt, :].bitcast(f32),
                                        ALU.subtract).then_inc(dve_lo_ready, 1)

            def turn(c, u, it):
                places = PHASES[phase_of(c)]
                owed = None
                for k, pair in enumerate(places):
                    if pair is not None:
                        layer, tiles, mode, ahead = pair
                        rows, nt, i = rows_of(layer), len(tiles), ring(u, ahead)
                        b, p = slot(u, k, BC_SLOTS), slot(u, k, PROD_SLOTS)
                        dve.wait_ge(bc_ready, done(c, k + 1))
                        if layer == 0:
                            dve.wait_ge(x_rot_loaded[i][tiles[0] // 2], filling(u, it, ahead) * (16 * nt))
                        if layer == 1 and tiles[0] == 0:
                            dve.wait_ge(h_ready, c + 1)
                        if mode != DVE:
                            user = last_user(c, k, PROD_SLOTS, (POOL, NATIVE))
                            if user is not None and user[2] == POOL:
                                dve.wait_ge(pool_lo_ready, done(user[0], user[1] + 1, (POOL,)))
                            elif user is not None:
                                dve.wait_ge(pair_done, done(user[0], user[1] + 1))
                        to = bc[:rows, b, :nt, :] if mode == DVE else prod[:rows, p, :nt, :]
                        if layer:
                            repeated = bc[:rows, b, :nt, :]
                            other = h[:rows, i, :].unsqueeze(1).broadcast_to([rows, nt, NC])
                        else:
                            repeated = bc[:rows, b, nt - 1, :].unsqueeze(1).broadcast_to([rows, nt, NC])
                            other = x_rot[:rows, rot_slot(1 + u + ahead, tiles[0] // 2), :nt, :]
                        nc.vector.tensor_tensor(to, repeated, other, ALU.mult).then_inc(prod_ready, 1)
                    if owed is not None:
                        low(c, u, owed, *places[owed][:2])
                    owed = k if pair is not None and pair[2] == DVE else None
                    if owed is not None and (k + 1 == PLACES or places[k + 1] is None):
                        low(c, u, owed, *places[owed][:2])
                        owed = None
                    if k == FIRST_REDUCE0_AT and isinstance(c, int) and c == 0:
                        reduce0(0, 0)
                    if k == REDUCE0_AT and has_layer0(c) and not starts(c):
                        y0_chunk = reduce0(c + 1, ring(u, 1))
                        if isinstance(c, int) and c == CHUNKS - 2:
                            y0_chunk.then_inc(y0_ready, 1)
                    if k == REDUCE1_AT and has_before(c):
                        reduce1(c - 1, ring(u, -1))
                if isinstance(c, int) and c == CHUNKS - 1:
                    reduce1(c, ring(u)).then_inc(y1_ready, 1)

            turns(dve, turn)

        @block.tensor
        def _(pe):
            def broadcast(c, u, k):
                pair = PHASES[phase_of(c)][k]
                if pair is None:
                    return
                layer, tiles, mode, ahead = pair
                i, b = ring(u, ahead), slot(u, k, BC_SLOTS)
                if layer == 0 and tiles[0] == 0:
                    pe.wait_ge(x_half_ready, c + ahead + 1)
                if isinstance(c, int) and c == 0 and layer == 1 and tiles[0] == 0:
                    pe.wait_ge(sel_ready, 2)
                user = last_user(c, k, BC_SLOTS, WAYS)
                if user is not None and user[2] == DVE:
                    pe.wait_ge(dve_lo_ready, done(user[0], user[1] + 1, (DVE,)))
                elif user is not None:
                    pe.wait_ge(prod_ready, done(user[0], user[1] + 1))
                for e, which in enumerate([1 + t for t in tiles]) if layer else [(len(tiles) - 1, 0)]:
                    last = nc.tensor.matmul(bc[:rows_of(layer), b, e, :], sel[:, which, :rows_of(layer)],
                                            x_half[:, i, :], start=True, stop=True)
                last.then_inc(bc_ready, 1)

            def contract(c, u, k):
                pair = PHASES[phase_of(c)][k]
                if pair is None:
                    return
                layer, tiles, mode, ahead = pair
                rows, acc = rows_of(layer), acc1 if layer else acc0
                p, hi, lo = slot(u, k, PROD_SLOTS), slot(u, k, HI_SLOTS), slot(u, k, LO_SLOTS)
                first, final = tiles[0] == 0, tiles[-1] == (T1 if layer else T0) - 1
                if first and layer == 0:
                    if isinstance(c, int) and c + ahead == 0:
                        pe.wait_ge(w0_summed, 1)
                        pe.wait_ge(w_lo_ready, 1)
                    else:
                        pe.wait_ge(direct0_ready, c + ahead)
                if first and layer == 1:
                    if isinstance(c, int) and c == 0:
                        pe.wait_ge(w_lo_ready, 2)
                    else:
                        pe.wait_ge(direct1_ready, c)
                if mode == NATIVE:
                    pe.wait_ge(prod_ready, done(c, k + 1))
                    for e, t in enumerate(tiles):
                        last = nc.tensor.matmul(acc[:], w[:rows, layer * T0 + t, :], prod[:rows, p, e, :],
                                                start=(first and e == 0), stop=(final and e == len(tiles) - 1))
                else:
                    pe.wait_ge(hi_ready, done(c, k + 1, (POOL, DVE)))
                    for e, t in enumerate(tiles):
                        nc.tensor.matmul(acc[:], w_hi[:rows, layer * T0 + t, :], prod_hi[:rows, hi, e, :],
                                         start=(first and e == 0), stop=False)
                        nc.tensor.matmul(acc[:], w_lo[:rows, layer * T0 + t, :], prod_hi[:rows, hi, e, :],
                                         start=False, stop=False)
                    lo_ready = pool_lo_ready if mode == POOL else dve_lo_ready
                    pe.wait_ge(lo_ready, done(c, k + 1, (mode,)))
                    for e, t in enumerate(tiles):
                        last = nc.tensor.matmul(acc[:], w_hi[:rows, layer * T0 + t, :], prod_lo[:rows, lo, e, :],
                                                start=False, stop=(final and e == len(tiles) - 1))
                last.then_inc(pair_done, 1)

            pe.wait_ge(sel_ready, 1)

            def turn(c, u, it):
                start, lag = (PLACES - len(START), START_LAG) if starts(c) else (0, LAG)
                if starts(c):
                    for k in range(start, start + lag):
                        broadcast(c, u, k)
                for k in range(start, PLACES):
                    if k + lag < PLACES:
                        broadcast(c, u, k + lag)
                    elif not isinstance(c, int) or c < CHUNKS - 1:
                        broadcast(c + 1, u + 1, k + lag - PLACES)
                    contract(c, u, k)
                if starts(c):
                    for k in range(lag, LAG):
                        broadcast(c + 1, u + 1, k)

            turns(pe, turn)


def kernel(r_x, L0_rec_W0, L0_rec_b0, L0_rec_W1, L0_rec_b1):
    import concourse.bacc as bacc
    from concourse.bass_utils import run_bass_kernel_spmd

    f32 = mybir.dt.float32
    x, w0, w1 = np.asarray(r_x), np.asarray(L0_rec_W0), np.asarray(L0_rec_W1)
    p, q = np.ogrid[:K0, :T0]
    i = p // ROT + 0 * q
    j = (i + ROT * q + p % ROT) % F
    sel, flags = sel_tables()
    b0, b1 = np.asarray(L0_rec_b0), np.asarray(L0_rec_b1)
    arrays = {
        "x_dram": np.ascontiguousarray(x.transpose(1, 0, 2).reshape(F, N)[np.arange(F + ROT * T0 - 1) % F]),
        "w0_ij_dram": np.ascontiguousarray(w0[i, j]),
        "w0_ji_dram": np.ascontiguousarray(w0[j, i]),
        "w1_dram": np.ascontiguousarray(w1.reshape(T1, K1, S1).transpose(1, 0, 2)),
        "sel_dram": sel,
        "columns_dram": np.concatenate([flags, np.stack([b0, np.tile(b0[:HALF], 2), b1], 1)], 1),
    }
    nc = bacc.Bacc("TRN2", target_bir_lowering=False, num_devices=1)
    d = {k: nc.dram_tensor(k, v.shape, f32, kind="ExternalInput").ap() for k, v in arrays.items()}
    y = nc.dram_tensor("y_dram", (S0 - HALF + S1, B), f32, kind="ExternalOutput").ap()
    build(nc, d["x_dram"], d["w0_ij_dram"], d["w0_ji_dram"], d["w1_dram"], d["sel_dram"],
          d["columns_dram"], y)
    r = run_bass_kernel_spmd(nc, [arrays], core_ids=[0])
    return np.ascontiguousarray(r.results[0]["y_dram"].T)
```
